# Optimizing a Trainium2 kernel written in Bass

```python
import numpy as np
import jax
import jax.numpy as jnp

def _softmax(x, axis=-1):
    return jax.nn.softmax(x, axis=axis)
def _gelu(x):
    return jax.nn.gelu(x, approximate=True)
def _silu(x):
    return jax.nn.silu(x)
def _sigmoid(x):
    return jax.nn.sigmoid(x)
def _layernorm(x, axis=-1, eps=1e-5):
    m = jnp.mean(x, axis=axis, keepdims=True)
    v = jnp.var(x, axis=axis, keepdims=True)
    return (x - m) / jnp.sqrt(v + eps)
def _scatter_add(tgt, idx, src, axis=0):
    return tgt.at[idx].add(src)
def _segment_sum(src, seg, n):
    return jax.ops.segment_sum(src, seg, n)

kernel_name = 'mk_conv_preact_d2_conv_nchw8_467efe'

def setup_inputs(seed: int = 0):
    np.random.seed(seed)
    _w = jnp.asarray
    def _rec_inputs():
        import jax
        import jax.numpy as jnp
        _gk = jax.random.key(seed)
        x = -9.629e-05 + 1 * jax.random.normal(jax.random.fold_in(_gk, 1), (8, 8, 1024, 1024), jnp.float32)
        return x
    x = _rec_inputs()
    def _L0_conv_setup():
        import jax, jax.numpy as jnp
        import numpy as np
        import math
        B, C_IN, C_OUT = (32, 8, 8)
        H, W = (1024, 1024)
        KH, KW = (3, 3)
        STRIDE = 1
        PAD = 1
        key = jax.random.key(seed)
        k1, k2, k3 = jax.random.split(key, 3)
        stdv = math.sqrt(1.0 / (C_IN * KH * KW))
        x = jax.random.normal(k1, (B, C_IN, H, W), dtype=jnp.float32)
        weight = jax.random.uniform(k2, (C_OUT, C_IN, KH, KW), dtype=jnp.float32, minval=-stdv, maxval=stdv)
        bias = jax.random.uniform(k3, (C_OUT,), dtype=jnp.float32, minval=-stdv, maxval=stdv)
        return {'input': x, 'weight': weight, 'bias': bias}
    _L0_conv_all = _L0_conv_setup()
    _L0_conv_in = {k: v for k, v in _L0_conv_all.items() if k in ('weight', 'bias', )}
    del _L0_conv_all

    def _L1_conv_setup():
        import jax, jax.numpy as jnp
        import numpy as np
        import math
        B, C_IN, C_OUT = (32, 8, 8)
        H, W = (1024, 1024)
        KH, KW = (3, 3)
        STRIDE = 1
        PAD = 1
        key = jax.random.key(seed)
        k1, k2, k3 = jax.random.split(key, 3)
        stdv = math.sqrt(1.0 / (C_IN * KH * KW))
        x = jax.random.normal(k1, (B, C_IN, H, W), dtype=jnp.float32)
        weight = jax.random.uniform(k2, (C_OUT, C_IN, KH, KW), dtype=jnp.float32, minval=-stdv, maxval=stdv)
        bias = jax.random.uniform(k3, (C_OUT,), dtype=jnp.float32, minval=-stdv, maxval=stdv)
        return {'input': x, 'weight': weight, 'bias': bias}
    _L1_conv_all = _L1_conv_setup()
    _L1_conv_in = {k: v for k, v in _L1_conv_all.items() if k in ('weight', 'bias', )}
    del _L1_conv_all

    return {
        "x": x,
        "L0_conv_weight": _L0_conv_in["weight"],
        "L0_conv_bias": _L0_conv_in["bias"],
        "L1_conv_weight": _L1_conv_in["weight"],
        "L1_conv_bias": _L1_conv_in["bias"],
    }

def reference(x, L0_conv_weight, L0_conv_bias, L1_conv_weight, L1_conv_bias):
    import jax
    import jax.numpy as jnp
    def _L0_conv_ref(input, weight, bias):
        import jax, jax.numpy as jnp
        import numpy as np
        import math
        B, C_IN, C_OUT = (32, 8, 8)
        H, W = (1024, 1024)
        KH, KW = (3, 3)
        STRIDE = 1
        PAD = 1
        out = jax.lax.conv_general_dilated(input, weight, window_strides=(STRIDE, STRIDE), padding=[(PAD, PAD), (PAD, PAD)], dimension_numbers=('NCHW', 'OIHW', 'NCHW'))
        return out + bias[None, :, None, None]

    def _L1_conv_ref(input, weight, bias):
        import jax, jax.numpy as jnp
        import numpy as np
        import math
        B, C_IN, C_OUT = (32, 8, 8)
        H, W = (1024, 1024)
        KH, KW = (3, 3)
        STRIDE = 1
        PAD = 1
        out = jax.lax.conv_general_dilated(input, weight, window_strides=(STRIDE, STRIDE), padding=[(PAD, PAD), (PAD, PAD)], dimension_numbers=('NCHW', 'OIHW', 'NCHW'))
        return out + bias[None, :, None, None]

    def _gn(v, G=4, eps=1e-5):
        B_, C_, H_, W_ = v.shape
        g = v.reshape(B_, G, C_ // G, H_, W_)
        m = jnp.mean(g, axis=(2, 3, 4), keepdims=True)
        s = jnp.var(g, axis=(2, 3, 4), keepdims=True)
        return ((g - m) / jnp.sqrt(s + eps)).reshape(v.shape)

    def _ln_c(v, eps=1e-6):
        m = jnp.mean(v, axis=1, keepdims=True)
        s = jnp.var(v, axis=1, keepdims=True)
        return (v - m) / jnp.sqrt(s + eps)

    def _ln_t(v, eps=1e-5):
        m = jnp.mean(v, axis=-1, keepdims=True)
        s = jnp.var(v, axis=-1, keepdims=True)
        return (v - m) / jnp.sqrt(s + eps)

    def _to_tokens(v):
        B_, C_, H_, W_ = v.shape
        return v.reshape(B_, C_, H_ * W_).transpose(0, 2, 1)
    def _from_tokens(t, like):
        B_, C_, H_, W_ = like.shape
        return t.transpose(0, 2, 1).reshape(B_, C_, H_, W_)

    x = x + _L0_conv_ref(_gn(x), L0_conv_weight, L0_conv_bias)
    x = x + _L1_conv_ref(_gn(x), L1_conv_weight, L1_conv_bias)
    return x


_drawn_inputs = setup_inputs


def setup_inputs(seed=0):
    import zlib

    import numpy as np

    out = dict(_drawn_inputs(seed))
    spreads = {}
    factors = {}
    for name, (base, spread) in spreads.items():
        noise = np.random.default_rng([zlib.crc32(name.encode()), seed]).standard_normal(out[name].shape)
        drawn = base * np.exp(spread * noise) if base else spread * noise
        out[name] = jnp.asarray(drawn.astype(out[name].dtype))
    for name, factor in factors.items():
        out[name] = (out[name] * factor).astype(out[name].dtype)
    return out
```

```python
from contextlib import ExitStack

import numpy as np

import concourse.bass as bass
from concourse import mybir

P = 128
KW = 3
EDGE_FIRST, EDGE_LAST, INNER = 6, 7, 0
RING = 6
SLOTS = RING + 2
PSUM_RING = 3
LAG_OUT = 2
LAG_STORE = 3
STATS_FROM = 3
EPS = 1e-5


def sizes(B, C, H, W):
    rows_in = P // C
    rows_out = rows_in - 2
    T = (H - 2) // rows_out + 1
    assert H == (T - 1) * rows_out + 2 and (T - 2) % RING == 0
    chunks = T - 10
    chunk_cols = C * H * W // (P * chunks)
    assert chunk_cols * P * chunks == C * H * W and chunks % 4 == 0
    units = next(u for u in range(1, chunk_cols) if chunk_cols // u <= 512 and chunk_cols % (2 * u) == 0)
    return rows_in, rows_out, T, chunks, chunk_cols, units


def layout_constants(C, H, W, G):
    rows_in, rows_out, T, *_ = sizes(2, C, H, W)
    p = np.arange(P)
    row, ch = p // C, p % C
    group = ch // (C // G)
    band = np.zeros((P, 3, rows_in, C), np.float32)
    for kh in range(3):
        for ro in range(rows_in):
            band[:, kh, ro, :] = (row == ro + kh - 1)[:, None]
    same = group[:, None] == group[None, :]
    count = (C // G) * H * W
    body = same * ((row >= 1) & (row <= rows_out))[:, None] * ((T - 1) * W / count)
    last = same * ((row >= 1) & (row <= 2))[:, None] * (W / count)
    average = np.full((P, P), 1.0 / P)
    member = group[:, None] == np.arange(G)[None, :]
    minus = -np.stack([np.ones(P), row >= 1, row <= 2], 1)
    return np.concatenate([band.reshape(P, -1), body, last, average, member, minus], 1).astype(np.float32)


def place(t, T):
    return EDGE_FIRST if t == 0 else EDGE_LAST if t == T - 1 else (t - 1) % RING


def psum_place(t, T):
    return 2 if t == 0 else 0 if t == T - 1 else (t - 1) % PSUM_RING


def build(nc, x, w0, b0, w1, b1, consts, mid, out):
    f32, f32r = mybir.dt.float32, mybir.dt.float32r
    ALU, ACT, AX = mybir.AluOpType, mybir.ActivationFunctionType, mybir.AxisListType
    B, C, H, W = x.shape
    G = 4
    R, RO, T, CHUNKS, CHUNK, UNITS = sizes(B, C, H, W)
    USES = (T - 2) // RING
    HALF = W // 2
    NTAP = R * C
    UNIT = CHUNK // UNITS
    GCOLS = CHUNKS // G * UNITS * 6

    x_chunks = x.rearrange("b c h w -> b (c h w)").rearrange("b (k p n) -> b k p n", p=P, n=CHUNK)

    ctx = ExitStack()
    with ctx:
        def sb(name, shape, dt=f32):
            return ctx.enter_context(nc.sbuf_tensor(name, shape, dt))

        def sem(name):
            return ctx.enter_context(nc.semaphore(name))

        x_t = sb("x_t", [P, SLOTS, W])
        hi = sb("hi", [P, SLOTS, W + 2], f32r)
        lo = sb("lo", [P, SLOTS, W + 2], f32r)
        out_t = sb("out_t", [P, SLOTS, W])
        chunk_t = sb("chunk_t", [P, RING, CHUNK])
        const_t = sb("const_t", [P, consts.shape[1]])
        w_raw = sb("w_raw", [P, 2, C, 9])
        bias_t = sb("bias_t", [P, 2])
        w_tap = sb("w_tap", [P, 3, NTAP])
        w_band = sb("w_band", [P, 2, KW, NTAP])
        w_scaled = sb("w_scaled", [P, KW, NTAP])
        w_hi = sb("w_hi", [P, 2, KW, NTAP], f32r)
        w_lo = sb("w_lo", [P, 2, KW, NTAP], f32r)
        x_stats = sb("x_stats", [P, G * GCOLS])
        y_stats = sb("y_stats", [P, T * 12])
        x_agg = sb("x_agg", [P, G, 2])
        y_agg = sb("y_agg", [P, 2, 2])
        c_mean = sb("c_mean", [P, G])
        c_a = sb("c_a", [P, G])
        c_b = sb("c_b", [P, G])
        c_var = sb("c_var", [P, G])
        c_r = sb("c_r", [P, 2 * G])
        wait_cell = sb("wait_cell", [P, 1])
        rstd = sb("rstd", [P, 1])
        mean = sb("mean", [P, 1])
        shift = sb("shift", [P, 2, 3])

        conv = [ctx.enter_context(nc.psum_tensor(f"conv{i}", [P, W], f32)) for i in range(PSUM_RING)]
        small = ctx.enter_context(nc.psum_tensor("small", [P, 512], f32))

        band = const_t[:, 0:3 * NTAP].rearrange("p (k r c) -> p k r c", k=3, c=C)
        avg_body = const_t[:, 3 * NTAP:3 * NTAP + P]
        avg_last = const_t[:, 3 * NTAP + P:3 * NTAP + 2 * P]
        avg_all = const_t[:, 3 * NTAP + 2 * P:3 * NTAP + 3 * P]
        member = const_t[:, 3 * NTAP + 3 * P:3 * NTAP + 3 * P + G]
        minus = const_t[:, 3 * NTAP + 3 * P + G:3 * NTAP + 3 * P + G + 3]

        consts_landed = sem("consts_landed")
        zeroed = sem("zeroed")
        prep = sem("prep")
        x_landed = [sem(f"x_landed{s}") for s in range(SLOTS)]
        chunk_landed = [sem(f"chunk_landed{s}") for s in range(RING)]
        chunk_read = sem("chunk_read")
        hi_ready = sem("hi_ready")
        lo_ready = sem("lo_ready")
        conv_done = sem("conv_done")
        out_ready = sem("out_ready")
        stored = [sem(f"stored{s}") for s in range(SLOTS)]
        y_stats_done = sem("y_stats_done")
        y_agg_done = sem("y_agg_done")
        x_chain = sem("x_chain")
        y_chain = sem("y_chain")
        coef_sum = sem("coef_sum")
        root_ready = sem("root_ready")
        coef_ready = sem("coef_ready")

        X_AGG, X_VAR, X_LEN = G, G + 4, G + 16
        Y_VAR, Y_LEN = 4, 12

        def phases(eng, phase):
            phase(0, 0, 0, 1, None, (0, 1))
            phase(1, 0, 1, None, (0, 0), (1, 0))
            with eng.Fori(0, B - 2) as i:
                phase(2 * i + 2, 1, i, i + 2, (0, i + 1), (0, i + 2))
                phase(2 * i + 3, 0, i + 2, None, (1, i), (1, i + 1))
            phase(2 * B - 2, 1, B - 2, None, (0, B - 1), (1, B - 1))
            phase(2 * B - 1, 1, B - 1, None, (1, B - 2), None)

        def steps(eng, step, ph=1):
            head = 7 + RING if isinstance(ph, int) and ph == 0 else 7
            for t in range(head):
                step(t, t, 0)
            with eng.Fori(0, (T - 7 - head) // RING) as k:
                for j in range(head, head + RING):
                    step(k * RING + j, j, k)
            for t in range(T - 7, T):
                step(t, t, 0)

        def ago(j, d):
            return j - d if j >= d else j - d + T

        def uses(ph, j, k):
            return ph if j in (0, T - 1) else ph * USES + (j - 1) // RING + k

        def positive(v):
            return not isinstance(v, int) or v > 0

        def ring_back(j):
            return RING + 2 if 1 <= j <= RING else RING

        def chunk_arrivals(image, j, k):
            ahead = 1 if (j - 1) % RING >= 2 else 0
            earlier = (j - 3) // RING if ahead else (j - 7) // RING
            return image * (CHUNKS // RING + ahead) + earlier + k + 1

        block = ctx.enter_context(nc.Block())

        @block.sync
        def _(sp):
            sp.dma_start(const_t[:, :], consts).then_inc(consts_landed, 16)
            for layer, (w, b) in enumerate([(w0, b0), (w1, b1)]):
                w_v = w.rearrange("o i kh kw -> i o (kh kw)")
                b_v = b.rearrange("(c u) -> c u", u=1)
                for r in range(R):
                    sp.dma_start(w_raw[C * r:C * r + C, layer], w_v).then_inc(consts_landed, 16)
                    sp.dma_start(bias_t[C * r:C * r + C, layer:layer + 1], b_v).then_inc(consts_landed, 16)
            sp.wait_ge(zeroed, 1)

            def load_chunk(image, t, j, k):
                if STATS_FROM <= j < STATS_FROM + CHUNKS:
                    back = {3: 4, 4: 4, 5: 4, 6: 4, 7: 4, 8: 5}.get(j, RING)
                    free = image * CHUNKS + t - STATS_FROM - back + 1
                    if positive(free):
                        sp.wait_ge(chunk_read, free)
                    s = (j - 1) % RING
                    sp.dma_start(chunk_t[:, s, :], x_chunks[image, t - STATS_FROM]).then_inc(chunk_landed[s], 16)

            steps(sp, lambda t, j, k: load_chunk(0, t, j, k))

            def phase(ph, layer, image, stats_image, before, after):
                if layer == 1:
                    for s in range(SLOTS):
                        sp.wait_ge(stored[s], 16 * (ph - 1) * (USES if s < RING else 1))

                def step(t, j, k):
                    n = ph * T + t
                    s = place(j, T)
                    if s < RING and positive(n - ring_back(j) + 1):
                        sp.wait_ge(out_ready, n - ring_back(j) + 1)
                    if layer == 0:
                        def rows(h, m):
                            return x[image, :, bass.ds(h, m), :].rearrange("c r w -> r c w")
                    else:
                        def rows(h, m):
                            return mid[image, bass.ds(h, m), :, :]
                    if j == 0:
                        sp.dma_start(x_t[C:P, s, :], rows(0, R - 1)).then_inc(x_landed[s], 16)
                    elif j == T - 1:
                        sp.dma_start(x_t[0:3 * C, s, :], rows(H - 3, 3)).then_inc(x_landed[s], 16)
                    else:
                        sp.dma_start(x_t[:, s, :], rows(t * RO - 1, R)).then_inc(x_landed[s], 16)
                    if stats_image is not None:
                        load_chunk(stats_image, t, j, k)

                steps(sp, step, ph)

            phases(sp, phase)

        @block.gpsimd
        def _(pool):
            nc.gpsimd.memset(x_t[:, EDGE_FIRST:SLOTS, :], 0.0)
            nc.gpsimd.memset(hi[:, :, 0:1].bitcast(f32), 0.0)
            nc.gpsimd.memset(hi[:, :, W + 1:W + 2].bitcast(f32), 0.0)
            nc.gpsimd.memset(lo[:, :, 0:1].bitcast(f32), 0.0)
            nc.gpsimd.memset(lo[:, :, W + 1:W + 2].bitcast(f32), 0.0).then_inc(zeroed, 1)

        @block.scalar
        def _(act):
            def store(ph, layer, image, t, j):
                s = place(j, T)
                if layer == 0:
                    def rows(h, m):
                        return mid[image, bass.ds(h, m), :, :]
                else:
                    def rows(h, m):
                        return out[image, :, bass.ds(h, m), :].rearrange("c r w -> r c w")
                act.wait_ge(out_ready, ph * T + t + 1)
                if j == T - 1:
                    act.dma_start(rows(H - 2, 2), out_t[C:3 * C, s, :]).then_inc(stored[s], 16)
                else:
                    act.dma_start(rows(t * RO, RO), out_t[C:C + RO * C, s, :]).then_inc(stored[s], 16)

            def root(layer, image):
                w = G if layer == 0 else 1
                if layer == 0:
                    act.wait_ge(x_chain, X_LEN * image + X_VAR + 1)
                else:
                    act.wait_ge(y_chain, Y_LEN * image + Y_VAR + 1)
                nc.scalar.activation(c_r[:, G:G + w], c_a[:, 0:w], ACT.Sqrt).then_inc(root_ready, 1)

            def phase(ph, layer, image, stats_image, before, after):
                act.wait_ge(coef_ready, ph + 1)
                parity = 0 if ph is None else phase_parity(ph, layer, B)

                def step(t, j, k):
                    s = place(j, T)
                    n = ph * T + t
                    act.wait_ge(x_landed[s], 16 * (uses(ph, j, k) + 1))
                    if s < RING and positive(n - ring_back(j) + 1):
                        act.wait_ge(conv_done, n - ring_back(j) + 1)
                    v = 1 if j == 0 else 2 if j == T - 1 else 0
                    nc.scalar.activation(hi[:, s, 1:W + 1], x_t[:, s, :], ACT.Identity,
                                         bias=shift[:, parity, v:v + 1], scale=1.0).then_inc(hi_ready, 1)
                    if j >= LAG_STORE:
                        store(ph, layer, image, t - LAG_STORE, j - LAG_STORE)
                    elif before is not None:
                        q = ago(j, LAG_STORE)
                        store(ph - 1, before[0], before[1], q, q)
                    if after is not None and j == T - 3:
                        root(*after)

                steps(act, step, ph)

            root(0, 0)
            phases(act, phase)
            for t in range(T - LAG_STORE, T):
                store(2 * B - 1, 1, B - 1, t, t)
            for s in range(SLOTS):
                act.wait_ge(stored[s], 16 * 2 * B * (USES if s < RING else 1))

        @block.vector
        def _(dve):
            dve.wait_ge(consts_landed, 16 * (1 + 4 * R))
            dve.wait_ge(zeroed, 1)
            count = 0
            for layer in range(2):
                w_v = w_raw[:, layer].rearrange("p o (kh kw) -> p o kh kw", kw=KW)
                for kh in range(3):
                    if count:
                        dve.wait_ge(prep, count)
                    for kw in range(KW):
                        a = w_v[:, :, kh, kw].unsqueeze(1).broadcast_to([P, R, C])
                        dst = w_tap[:, kw, :] if kh else w_band[:, layer, kw, :]
                        tap = dst.rearrange("p (r c) -> p r c", c=C)
                        last = nc.vector.tensor_tensor(tap, a, band[:, kh], ALU.mult)
                    last.then_inc(prep, 1)
                    count += 1
                    if kh:
                        dve.wait_ge(prep, count)
                        nc.vector.tensor_tensor(w_band[:, layer], w_band[:, layer], w_tap[:, :, :],
                                                ALU.add).then_inc(prep, 1)
                        count += 1

            def chunk_stats(image, t, j, k):
                if STATS_FROM <= j < STATS_FROM + CHUNKS:
                    s = (j - 1) % RING
                    dve.wait_ge(chunk_landed[s], 16 * chunk_arrivals(image, j, k))
                    for u in range(UNITS):
                        last = nc.vector.bn_stats(
                            x_stats[:, bass.ds(((t - STATS_FROM) * UNITS + u) * 6, 6)],
                            chunk_t[:, s, u * UNIT:(u + 1) * UNIT])
                    last.then_inc(chunk_read, 1)

            def aggregate_x(image):
                dve.wait_ge(chunk_read, (image + 1) * CHUNKS)
                nc.vector.memset(wait_cell[:, :], 0.0)
                for g in range(G):
                    nc.vector.bn_aggr(x_agg[:, g, :],
                                      x_stats[:, g * GCOLS:(g + 1) * GCOLS]).then_inc(x_chain, 1)

            def aggregate_y(image):
                dve.wait_ge(y_stats_done, (image + 1) * T * 2)
                nc.vector.memset(wait_cell[:, :], 0.0)
                nc.vector.bn_aggr(y_agg[:, 0, :], y_stats[:, 0:(T - 1) * 12]).then_inc(y_agg_done, 1)
                nc.vector.bn_aggr(y_agg[:, 1, :], y_stats[:, (T - 1) * 12:T * 12]).then_inc(y_agg_done, 1)
                dve.wait_ge(y_agg_done, 2 * image + 2)

            def variances(layer, image, ph):
                chain, length, at = (x_chain, X_LEN, X_AGG) if layer == 0 else (y_chain, Y_LEN, 0)
                dve.wait_ge(coef_sum, 2 * ph + 1)
                if layer == 0:
                    means, varis, m, n = x_agg[:, :, 0], x_agg[:, :, 1], small[:, 0:G], G
                else:
                    means, varis, m, n = y_agg[:, :, 0], y_agg[:, :, 1], small[:, 0:1], 2
                w = G if layer == 0 else 1
                nc.vector.tensor_copy(c_mean[:, 0:w], m).then_inc(chain, 1)
                at += 1
                dve.wait_ge(chain, length * image + at)
                if layer == 0:
                    nc.vector.tensor_tensor(c_a[:, 0:n], means, c_mean[:, 0:n], ALU.subtract).then_inc(chain, 1)
                else:
                    nc.vector.tensor_scalar(c_a[:, 0:n], means, c_mean[:, 0:1], None,
                                            ALU.subtract).then_inc(chain, 1)
                at += 1
                dve.wait_ge(chain, length * image + at)
                nc.vector.tensor_tensor(c_b[:, 0:n], c_a[:, 0:n], c_a[:, 0:n], ALU.mult).then_inc(chain, 1)
                at += 1
                dve.wait_ge(chain, length * image + at)
                nc.vector.tensor_tensor(c_var[:, 0:n], c_b[:, 0:n], varis, ALU.add).then_inc(chain, 1)

            def coefficients(layer, image, ph, parity):
                chain, length, at = (x_chain, X_LEN, X_VAR) if layer == 0 else (y_chain, Y_LEN, Y_VAR)
                w = G if layer == 0 else 1
                at = [at]

                def link(ins):
                    ins.then_inc(chain, 1)
                    at[0] += 1
                    dve.wait_ge(chain, length * image + at[0])

                dve.wait_ge(coef_sum, 2 * ph + 2)
                v, r, q = c_a[:, 0:w], c_r[:, 0:w], c_b[:, 0:w]
                link(nc.vector.tensor_scalar(v, small[:, G:G + w], EPS, None, ALU.add))
                dve.wait_ge(root_ready, ph + 1)
                link(nc.vector.reciprocal(r, c_r[:, G:G + w]))
                link(nc.vector.tensor_tensor(q, r, r, ALU.mult))
                link(nc.vector.tensor_tensor(c_var[:, 0:w], q, v, ALU.mult))
                link(nc.vector.tensor_scalar(q, c_var[:, 0:w], -0.5, 1.5, ALU.mult, ALU.add))
                if layer == 0:
                    link(nc.vector.tensor_tensor(c_a[:, :], r, q, ALU.mult))
                    link(nc.vector.tensor_tensor(c_b[:, :], c_a[:, :], member, ALU.mult))
                    link(nc.vector.reduce_sum(rstd[:, :], c_b[:, :], AX.X))
                    link(nc.vector.tensor_tensor(c_a[:, :], c_mean[:, :], member, ALU.mult))
                    link(nc.vector.reduce_sum(mean[:, :], c_a[:, :], AX.X))
                    link(nc.vector.tensor_scalar(w_scaled[:, :, :], w_band[:, layer], rstd[:, 0:1], None, ALU.mult))
                    m = mean[:, 0:1]
                else:
                    link(nc.vector.tensor_tensor(rstd[:, :], r, q, ALU.mult))
                    link(nc.vector.tensor_scalar(w_scaled[:, :, :], w_band[:, layer], rstd[:, 0:1], None, ALU.mult))
                    m = c_mean[:, 0:1]
                nc.vector.tensor_scalar(shift[:, parity, :], minus, m, None, ALU.mult)
                link(nc.vector.tensor_copy(w_hi[:, parity], w_scaled[:, :, :]))
                nc.vector.tensor_tensor(w_lo[:, parity], w_scaled[:, :, :], w_hi[:, parity].bitcast(f32),
                                        ALU.subtract).then_inc(coef_ready, 1)
                assert at[0] == length, (at[0], length)

            steps(dve, lambda t, j, k: chunk_stats(0, t, j, k))
            dve.wait_ge(prep, count)
            aggregate_x(0)
            variances(0, 0, 0)
            coefficients(0, 0, 0, 0)

            def output(ph, layer, t, j, k):
                s = place(j, T)
                dve.wait_ge(conv_done, ph * T + t + 1)
                if positive(uses(ph, j, k)):
                    dve.wait_ge(stored[s], 16 * uses(ph, j, k))
                nc.vector.scalar_tensor_tensor(out_t[:, s, :], conv[psum_place(j, T)][:, :],
                                               bias_t[:, layer:layer + 1], x_t[:, s, :],
                                               ALU.add, ALU.add).then_inc(out_ready, 1)

            def output_stats(ph, t, j):
                s = place(j, T)
                dve.wait_ge(out_ready, ph * T + t + 1)
                for h in range(2):
                    nc.vector.bn_stats(y_stats[:, bass.ds(t * 12 + 6 * h, 6)],
                                       out_t[:, s, h * HALF:(h + 1) * HALF]).then_inc(y_stats_done, 1)

            def phase(ph, layer, image, stats_image, before, after):
                parity = phase_parity(ph, layer, B)

                def step(t, j, k):
                    s = place(j, T)
                    n = ph * T + t
                    v = 1 if j == 0 else 2 if j == T - 1 else 0
                    dve.wait_ge(hi_ready, n + 1)
                    nc.vector.scalar_tensor_tensor(lo[:, s, 1:W + 1], x_t[:, s, :], shift[:, parity, v:v + 1],
                                                   hi[:, s, 1:W + 1].bitcast(f32),
                                                   ALU.add, ALU.subtract).then_inc(lo_ready, 1)
                    if j >= LAG_OUT:
                        output(ph, layer, t - LAG_OUT, j - LAG_OUT, k)
                    elif before is not None:
                        q = ago(j, LAG_OUT)
                        output(ph - 1, before[0], q, q, 0)
                    if j >= LAG_STORE:
                        if j == LAG_STORE and before is not None and before[0] == 0:
                            aggregate_y(before[1])
                        if layer == 0:
                            output_stats(ph, t - LAG_STORE, j - LAG_STORE)
                    elif before is not None and before[0] == 0:
                        q = ago(j, LAG_STORE)
                        output_stats(ph - 1, q, q)
                    if stats_image is not None:
                        chunk_stats(stats_image, t, j, k)
                    if after is not None:
                        if j == T - 7 and after[0] == 0:
                            aggregate_x(after[1])
                        if j == T - 5:
                            variances(after[0], after[1], ph + 1)
                        if j == T - 3:
                            coefficients(after[0], after[1], ph + 1, 1 - parity)

                steps(dve, step, ph)

            phases(dve, phase)
            for t in range(T - LAG_OUT, T):
                output(2 * B - 1, 1, t, t, 0)

        @block.tensor
        def _(pe):
            def sum_means(layer, image):
                if layer == 0:
                    pe.wait_ge(x_chain, X_LEN * image + X_AGG)
                    nc.tensor.matmul(small[:, 0:G], avg_all, x_agg[:, :, 0], start=True,
                                     stop=True).then_inc(coef_sum, 1)
                else:
                    pe.wait_ge(y_agg_done, 2 * image + 2)
                    nc.tensor.matmul(small[:, 0:1], avg_body, y_agg[:, 0, 0:1], start=True, stop=False)
                    nc.tensor.matmul(small[:, 0:1], avg_last, y_agg[:, 1, 0:1], start=False,
                                     stop=True).then_inc(coef_sum, 1)

            def sum_variances(layer, image):
                if layer == 0:
                    pe.wait_ge(x_chain, X_LEN * image + X_VAR)
                    nc.tensor.matmul(small[:, G:2 * G], avg_all, c_var[:, :], start=True,
                                     stop=True).then_inc(coef_sum, 1)
                else:
                    pe.wait_ge(y_chain, Y_LEN * image + Y_VAR)
                    nc.tensor.matmul(small[:, G:G + 1], avg_body, c_var[:, 0:1], start=True, stop=False)
                    nc.tensor.matmul(small[:, G:G + 1], avg_last, c_var[:, 1:2], start=False,
                                     stop=True).then_inc(coef_sum, 1)

            sum_means(0, 0)
            sum_variances(0, 0)

            def phase(ph, layer, image, stats_image, before, after):
                parity = phase_parity(ph, layer, B)
                pe.wait_ge(coef_ready, ph + 1)

                def step(t, j, k):
                    s = place(j, T)
                    n = ph * T + t
                    free = n - 1 if j in (0, 1) else n - 2
                    if positive(free):
                        pe.wait_ge(out_ready, free)
                    pe.wait_ge(lo_ready, n + 1)
                    acc = conv[psum_place(j, T)]
                    terms = [(w, v, kw) for v, w in ((hi, w_hi), (hi, w_lo), (lo, w_hi)) for kw in range(KW)]
                    for i, (w, v, kw) in enumerate(terms):
                        for h in range(2):
                            last = nc.tensor.matmul(acc[:, h * HALF:(h + 1) * HALF], w[:, parity, kw, :],
                                                    v[:, s, h * HALF + kw:h * HALF + kw + HALF],
                                                    start=(i == 0), stop=(i == len(terms) - 1))
                    last.then_inc(conv_done, 1)
                    if after is not None:
                        if j == T - 7:
                            sum_means(*after)
                        if j == T - 5:
                            sum_variances(*after)

                steps(pe, step, ph)

            phases(pe, phase)


def phase_parity(ph, layer, B):
    if isinstance(ph, int):
        return ph % 2
    return 1 - layer


def kernel(x, L0_conv_weight, L0_conv_bias, L1_conv_weight, L1_conv_bias):
    import concourse.bacc as bacc
    from concourse.bass_utils import run_bass_kernel_spmd

    B, C, H, W = x.shape
    arrays = {
        "x": np.ascontiguousarray(x),
        "w0": np.ascontiguousarray(L0_conv_weight),
        "b0": np.ascontiguousarray(L0_conv_bias),
        "w1": np.ascontiguousarray(L1_conv_weight),
        "b1": np.ascontiguousarray(L1_conv_bias),
        "consts": layout_constants(C, H, W, 4),
    }
    nc = bacc.Bacc("TRN2", target_bir_lowering=False, num_devices=1)
    f32 = mybir.dt.float32
    args = [nc.dram_tensor(n, a.shape, f32, kind="ExternalInput").ap() for n, a in arrays.items()]
    mid = nc.dram_tensor("layer0_out", (B, H, C, W), f32).ap()
    out = nc.dram_tensor("out", (B, C, H, W), f32, kind="ExternalOutput").ap()
    build(nc, *args, mid, out)
    r = run_bass_kernel_spmd(nc, [arrays], core_ids=[0])
    return r.results[0]["out"]
```

```python
from contextlib import ExitStack

import numpy as np

import concourse.bass as bass
from concourse import mybir

P = 128
KW = 3
EDGE_FIRST, EDGE_LAST = 6, 7
RING = 6
SLOTS = RING + 2
PSUM_RING = 3
LAG_OUT = 2
LAG_STORE = 3
STATS_FROM = 3
STATS_RING = 3
WHOLE, HALF_A, HALF_B = range(3)
EPS = 1e-5
BODY, LAST = 0, 1
Q = 4


def sizes(B, C, H, W):
    rows_in = P // C
    rows_out = rows_in - 2
    T = (H - 2) // rows_out + 1
    assert H == (T - 1) * rows_out + 2 and (T - 2) % RING == 0
    chunks = T - 10
    chunk_cols = C * H * W // (P * chunks)
    assert chunk_cols * P * chunks == C * H * W and chunks % 4 == 0
    units = next(u for u in range(1, chunk_cols) if chunk_cols // u <= 512 and chunk_cols % (2 * u) == 0)
    return rows_in, rows_out, T, chunks, chunk_cols, units


def layout_constants(C, H, W, G):
    rows_in, rows_out, T, *_ = sizes(2, C, H, W)
    p = np.arange(P)
    row, ch = p // C, p % C
    group = ch // (C // G)
    quarter, q_row = p // (P // Q), p % (P // Q) // C
    band = np.zeros((2, 3, P, P), np.float32)
    for kh in range(3):
        band[BODY, kh] = row[:, None] == row[None, :] + kh - 1
        band[LAST, kh] = (quarter[:, None] == quarter[None, :]) & (q_row[:, None] == q_row[None, :] + kh - 1)
    band = band.transpose(2, 0, 1, 3)
    same = group[:, None] == group[None, :]
    count = (C // G) * H * W
    body = same * ((row >= 1) & (row <= rows_out))[:, None] * ((T - 1) * W / count)
    last = same * ((q_row >= 1) & (q_row <= 2))[:, None] * (W // Q / count)
    average = np.full((P, P), 1.0 / P)
    member = group[:, None] == np.arange(G)[None, :]
    in_last = q_row <= 2
    minus = -np.stack([np.ones(P), row >= 1, in_last, in_last & (quarter > 0), in_last & (quarter < Q - 1)], 1)
    center = np.zeros((P, KW, P))
    center[:, KW // 2] = np.eye(P)
    parts = [band.reshape(P, -1), center.reshape(P, -1), body, last, average, member, minus]
    return np.concatenate(parts, 1).astype(np.float32)


def place(t, T):
    return EDGE_FIRST if t == 0 else EDGE_LAST if t == T - 1 else (t - 1) % RING


def psum_place(t, T):
    return 2 if t == 0 else 0 if t == T - 1 else (t - 1) % PSUM_RING


def build(nc, x, w0, b0, w1, b1, consts, mid, out):
    f32, f32r = mybir.dt.float32, mybir.dt.float32r
    ALU, ACT, AX = mybir.AluOpType, mybir.ActivationFunctionType, mybir.AxisListType
    B, C, H, W = x.shape
    G = 4
    R, RO, T, CHUNKS, CHUNK, UNITS = sizes(B, C, H, W)
    USES = (T - 2) // RING
    HALF = W // 2
    NTAP = R * C
    UNIT = CHUNK // UNITS
    GCOLS = CHUNKS // G * UNITS * 6

    x_chunks = x.rearrange("b c h w -> b (c h w)").rearrange("b (k p n) -> b k p n", p=P, n=CHUNK)
    x_pairs = x.rearrange("b c h w -> b (c h w)").rearrange("b (k z p n) -> b k p z n", z=2, p=P, n=CHUNK)

    ctx = ExitStack()
    with ctx:
        def sb(name, shape, dt=f32):
            return ctx.enter_context(nc.sbuf_tensor(name, shape, dt))

        def sem(name):
            return ctx.enter_context(nc.semaphore(name))

        x_t = sb("x_t", [P, SLOTS, W])
        hi = sb("hi", [P, SLOTS, W + 2], f32r)
        lo = sb("lo", [P, SLOTS, W + 2], f32r)
        out_t = sb("out_t", [P, SLOTS, W])
        chunk_t = sb("chunk_t", [P, STATS_RING, 2, CHUNK])
        const_t = sb("const_t", [P, consts.shape[1]])
        w_raw = sb("w_raw", [P, 2, C, 9])
        bias_t = sb("bias_t", [P, 2])
        w_tap = sb("w_tap", [P, KW * NTAP])
        w_band = sb("w_band", [P, 2, 2, KW * NTAP])
        w_scaled = sb("w_scaled", [P, 2, KW * NTAP])
        w_hi = sb("w_hi", [P, 2, 2, KW * NTAP], f32r)
        w_lo = sb("w_lo", [P, 2, 2, KW * NTAP], f32r)
        x_stats = sb("x_stats", [P, G * GCOLS])
        y_stats = sb("y_stats", [P, (T - 1) * 12 + 6])
        x_agg = sb("x_agg", [P, G, 2])
        y_agg = sb("y_agg", [P, 2, 2])
        c_mean = sb("c_mean", [P, G])
        c_a = sb("c_a", [P, G])
        c_b = sb("c_b", [P, G])
        c_var = sb("c_var", [P, G])
        c_r = sb("c_r", [P, 2 * G])
        wait_cell = sb("wait_cell", [P, 1])
        rstd = sb("rstd", [P, 1])
        mean = sb("mean", [P, 1])
        shift = sb("shift", [P, 2, 5])
        out_bias = sb("out_bias", [P, 2])

        conv = [ctx.enter_context(nc.psum_tensor(f"conv{i}", [P, W], f32)) for i in range(PSUM_RING)]
        small = ctx.enter_context(nc.psum_tensor("small", [P, 512], f32))

        band = const_t[:, 0:6 * NTAP].rearrange("p (z k r c) -> p z k r c", z=2, k=3, c=C)
        center = const_t[:, 6 * NTAP:9 * NTAP].unsqueeze(1).broadcast_to([P, 2, KW * NTAP])
        at = 9 * NTAP
        avg_body, avg_last, avg_all = (const_t[:, at + P * i:at + P * i + P] for i in range(3))
        member = const_t[:, at + 3 * P:at + 3 * P + G]
        minus = const_t[:, at + 3 * P + G:at + 3 * P + G + 5]

        consts_landed = sem("consts_landed")
        zeroed = sem("zeroed")
        prep = sem("prep")
        x_landed = [sem(f"x_landed{s}") for s in range(SLOTS)]
        chunk_landed = [sem(f"chunk_landed{s}") for s in range(STATS_RING)]
        chunk_read = sem("chunk_read")
        hi_ready = sem("hi_ready")
        lo_ready = sem("lo_ready")
        conv_done = sem("conv_done")
        out_ready = sem("out_ready")
        stored = [sem(f"stored{s}") for s in range(SLOTS)]
        y_stats_done = sem("y_stats_done")
        y_agg_done = sem("y_agg_done")
        x_chain = sem("x_chain")
        y_chain = sem("y_chain")
        coef_sum = sem("coef_sum")
        root_ready = sem("root_ready")
        coef_ready = sem("coef_ready")

        PREP_LEN = 2 * 2 * 5
        X_AGG, X_VAR, X_LEN = G, G + 4, G + 17
        Y_VAR, Y_LEN = 4, 13

        def phases(eng, phase):
            def pair(i, last):
                phase(2 * i + 2, 1, i, (i + 2, HALF_B), (0, i + 1), (0, i + 2))
                phase(2 * i + 3, 0, i + 2, None if last else (i + 3, HALF_A), (1, i), (1, i + 1))

            phase(0, 0, 0, (1, WHOLE), None, (0, 1))
            phase(1, 0, 1, (2, HALF_A), (0, 0), (1, 0))
            with eng.Fori(0, B - 3) as i:
                pair(i, False)
            pair(B - 3, True)
            phase(2 * B - 2, 1, B - 2, None, (0, B - 1), (1, B - 1))
            phase(2 * B - 1, 1, B - 1, None, (1, B - 2), None)

        def steps(eng, step, ph=1):
            head = 7 + RING if isinstance(ph, int) and ph == 0 else 7
            for t in range(head):
                step(t, t, 0)
            with nc.Fori(0, (T - 7 - head) // RING, engines=(eng.engine,), hint_back_edge=True) as k:
                for j in range(head, head + RING):
                    step(k * RING + j, j, k)
            for t in range(T - 7, T):
                step(t, t, 0)

        def ago(j, d):
            return j - d if j >= d else j - d + T

        def uses(ph, j, k):
            return ph if j in (0, T - 1) else ph * USES + (j - 1) // RING + k

        def moves(s):
            return Q if s == EDGE_LAST else 1

        QW = W // Q
        Y_COUNT = 2 * (T - 1) + 1

        def pieces(j):
            if j == T - 1:
                return [(3, 0, 1, 0), (4, QW + 1, QW + 2, QW + 1), (2, 1, QW + 1, 1)]
            return [(1 if j == 0 else 0, 1, W + 1, 0)]

        def positive(v):
            return not isinstance(v, int) or v > 0

        def ring_back(j):
            return RING + 2 if 1 <= j <= RING else RING

        def has_chunk(j):
            return STATS_FROM <= j < STATS_FROM + CHUNKS and (j - STATS_FROM) % 2 == 0

        def chunk_slot(j):
            return (j - 1) % RING // 2

        def turn(j, k):
            return (j - STATS_FROM) // 2 + STATS_RING * k

        def chunk_arrivals(n, j, k):
            ahead = 1 if chunk_slot(j) else 0
            earlier = (j - 3) // RING if ahead else (j - 7) // RING
            return n * (CHUNKS // RING + ahead) + earlier + k + 1

        block = ctx.enter_context(nc.Block())

        @block.sync
        def _(sp):
            def load_chunk(n, image, what, j, k):
                if has_chunk(j):
                    free = n * (CHUNKS // 2) + turn(j, k) - (2 if j < 7 else STATS_RING) + 1
                    if positive(free):
                        sp.wait_ge(chunk_read, free)
                    s, u = chunk_slot(j), turn(j, k)
                    if what == WHOLE:
                        to, src = chunk_t[:, s], x_pairs[image, u]
                    else:
                        to, src = chunk_t[:, s, 0], x_chunks[image, u + (CHUNKS // 2 if what == HALF_B else 0)]
                    sp.dma_start(to, src).then_inc(chunk_landed[s], 16)

            steps(sp, lambda t, j, k: load_chunk(0, 0, WHOLE, j, k), 0)

            def phase(ph, layer, image, stats, before, after):
                if layer == 1:
                    for s in (*range(RING), EDGE_FIRST):
                        sp.wait_ge(stored[s], 16 * (ph - 1) * (USES if s < RING else 1))

                def step(t, j, k):
                    n = ph * T + t
                    s = place(j, T)
                    if s < RING and positive(n - ring_back(j) + 1):
                        sp.wait_ge(lo_ready, n - ring_back(j) + 1)
                    if layer == 0:
                        def rows(h, m, c0=0, c1=W):
                            return x[image, :, bass.ds(h, m), c0:c1].rearrange("c r w -> r c w")
                    else:
                        def rows(h, m, c0=0, c1=W):
                            return mid[image, bass.ds(h, m), :, c0:c1].rearrange("r c w -> (r c) w")
                    if j == 0:
                        sp.dma_start(x_t[C:P, s, :], rows(0, R - 1)).then_inc(x_landed[s], 16)
                    elif j == T - 1:
                        if layer == 1:
                            sp.wait_ge(stored[s], 16 * moves(s) * (ph - 1))
                        for q in range(Q):
                            c0, c1 = max(q * QW - 1, 0), min(q * QW + QW + 1, W)
                            d = c0 - (q * QW - 1)
                            sp.dma_start(x_t[P // Q * q:P // Q * q + 3 * C, s, d:d + c1 - c0],
                                         rows(H - 3, 3, c0, c1)).then_inc(x_landed[s], 16)
                    else:
                        sp.dma_start(x_t[:, s, :], rows(t * RO - 1, R)).then_inc(x_landed[s], 16)
                    if stats is not None:
                        load_chunk(ph + 1, *stats, j, k)

                steps(sp, step, ph)

            sp.wait_ge(zeroed, 1)
            phases(sp, phase)

        @block.gpsimd
        def _(pool):
            nc.gpsimd.memset(x_t[:, EDGE_FIRST:SLOTS, :], 0.0)
            nc.gpsimd.memset(hi[:, :, 0:1].bitcast(f32), 0.0)
            nc.gpsimd.memset(hi[:, :, W + 1:W + 2].bitcast(f32), 0.0)
            nc.gpsimd.memset(lo[:, :, 0:1].bitcast(f32), 0.0)
            nc.gpsimd.memset(lo[:, :, W + 1:W + 2].bitcast(f32), 0.0).then_inc(zeroed, 1)

            pool.wait_ge(consts_landed, 16 * (1 + 4 * R))
            count = 0
            for layer in range(2):
                w_v = w_raw[:, layer].rearrange("p o (kh kw) -> p o kh kw", kw=KW)
                for kind in (BODY, LAST):
                    for kh in range(3):
                        if count:
                            pool.wait_ge(prep, count)
                        for kw in range(KW):
                            to = w_tap[:, kw * NTAP:(kw + 1) * NTAP] if kh else \
                                w_band[:, layer, kind, kw * NTAP:(kw + 1) * NTAP]
                            last = nc.gpsimd.tensor_tensor(
                                to.rearrange("p (r c) -> p r c", c=C),
                                w_v[:, :, kh, kw].unsqueeze(1).broadcast_to([P, R, C]),
                                band[:, kind, kh], ALU.mult)
                        last.then_inc(prep, 1)
                        count += 1
                        if kh:
                            pool.wait_ge(prep, count)
                            nc.gpsimd.tensor_tensor(w_band[:, layer, kind], w_band[:, layer, kind],
                                                    w_tap[:, :], ALU.add).then_inc(prep, 1)
                            count += 1
            assert count == PREP_LEN

        @block.scalar
        def _(act):
            act.dma_start(const_t[:, :], consts).then_inc(consts_landed, 16)
            for layer, (w, b) in enumerate([(w0, b0), (w1, b1)]):
                w_v = w.rearrange("o i kh kw -> i o (kh kw)")
                b_v = b.rearrange("(c u) -> c u", u=1)
                for r in range(R):
                    act.dma_start(w_raw[C * r:C * r + C, layer], w_v).then_inc(consts_landed, 16)
                    act.dma_start(bias_t[C * r:C * r + C, layer:layer + 1], b_v).then_inc(consts_landed, 16)

            def store(ph, layer, image, t, j):
                s = place(j, T)
                if layer == 0:
                    def rows(h, m, c0=0, c1=W):
                        return mid[image, bass.ds(h, m), :, c0:c1].rearrange("r c w -> (r c) w")
                else:
                    def rows(h, m, c0=0, c1=W):
                        return out[image, :, bass.ds(h, m), c0:c1].rearrange("c r w -> r c w")
                act.wait_ge(out_ready, ph * T + t + 1)
                if j == T - 1:
                    for q in range(Q):
                        p = P // Q * q + C
                        act.dma_start(rows(H - 2, 2, q * QW, q * QW + QW),
                                      out_t[p:p + 2 * C, s, 0:QW]).then_inc(stored[s], 16)
                else:
                    act.dma_start(rows(t * RO, RO), out_t[C:C + RO * C, s, :]).then_inc(stored[s], 16)

            def output(ph, layer, image, before, parity, t, j, k):
                s = place(j, T)
                if positive(uses(ph, j, k)):
                    act.wait_ge(stored[s], 16 * moves(s) * uses(ph, j, k))
                if j == 1 and before is not None and before[0] == 0:
                    act.wait_ge(y_stats_done, Y_COUNT * (before[1] + 1))
                if j > RING and s < RING and layer == 0:
                    act.wait_ge(y_stats_done, Y_COUNT * image + 2 * (t - RING + 1))
                act.wait_ge(conv_done, ph * T + t + 1)
                w = QW if j == T - 1 else W
                nc.scalar.activation(out_t[:, s, 0:w], conv[psum_place(j, T)][:, 0:w], ACT.Identity,
                                     bias=out_bias[:, parity:parity + 1], scale=1.0).then_inc(out_ready, 1)

            def root(layer, image):
                w = G if layer == 0 else 1
                if layer == 0:
                    act.wait_ge(x_chain, X_LEN * image + X_VAR + 1)
                else:
                    act.wait_ge(y_chain, Y_LEN * image + Y_VAR + 1)
                nc.scalar.activation(c_r[:, G:G + w], c_a[:, 0:w], ACT.Sqrt).then_inc(root_ready, 1)

            def phase(ph, layer, image, stats, before, after):
                act.wait_ge(coef_ready, ph + 1)
                parity = phase_parity(ph, layer)

                def step(t, j, k):
                    s = place(j, T)
                    n = ph * T + t
                    act.wait_ge(x_landed[s], 16 * moves(s) * (uses(ph, j, k) + 1))
                    if s < RING and positive(n - ring_back(j) + 1):
                        act.wait_ge(conv_done, n - ring_back(j) + 1)
                    for v, a, z, x_a in pieces(j):
                        last = nc.scalar.activation(hi[:, s, a:z], x_t[:, s, x_a:x_a + z - a], ACT.Identity,
                                                    bias=shift[:, parity, v:v + 1], scale=1.0)
                    last.then_inc(hi_ready, 1)
                    if j >= LAG_OUT:
                        output(ph, layer, image, before, parity, t - LAG_OUT, j - LAG_OUT, k)
                    elif before is not None:
                        q = ago(j, LAG_OUT)
                        output(ph - 1, before[0], before[1], None, 1 - parity, q, q, 0)
                    if j >= LAG_STORE:
                        store(ph, layer, image, t - LAG_STORE, j - LAG_STORE)
                    elif before is not None:
                        q = ago(j, LAG_STORE)
                        store(ph - 1, before[0], before[1], q, q)
                    if after is not None and j == T - 3:
                        root(*after)

                steps(act, step, ph)

            root(0, 0)
            phases(act, phase)
            for t in range(T - LAG_OUT, T):
                store(2 * B - 1, 1, B - 1, t - 1, t - 1)
                output(2 * B - 1, 1, B - 1, None, 1, t, t, 0)
            store(2 * B - 1, 1, B - 1, T - 1, T - 1)
            for s in range(SLOTS):
                act.wait_ge(stored[s], 16 * moves(s) * 2 * B * (USES if s < RING else 1))

        @block.vector
        def _(dve):
            def chunk_stats(n, what, j, k):
                if has_chunk(j):
                    s, u = chunk_slot(j), turn(j, k)
                    dve.wait_ge(chunk_landed[s], 16 * chunk_arrivals(n, j, k))
                    for z in range(2 if what == WHOLE else 1):
                        c = 2 * u + z if what == WHOLE else u + (CHUNKS // 2 if what == HALF_B else 0)
                        for i in range(UNITS):
                            last = nc.vector.bn_stats(x_stats[:, bass.ds((c * UNITS + i) * 6, 6)],
                                                      chunk_t[:, s, z, i * UNIT:(i + 1) * UNIT])
                    last.then_inc(chunk_read, 1)

            def aggregate_x(n):
                dve.wait_ge(chunk_read, (n + 1) * (CHUNKS // 2))
                nc.vector.memset(wait_cell[:, :], 0.0)
                for g in range(G):
                    nc.vector.bn_aggr(x_agg[:, g, :],
                                      x_stats[:, g * GCOLS:(g + 1) * GCOLS]).then_inc(x_chain, 1)

            def aggregate_y(image):
                dve.wait_ge(y_stats_done, (image + 1) * Y_COUNT)
                nc.vector.memset(wait_cell[:, :], 0.0)
                nc.vector.bn_aggr(y_agg[:, 0, :], y_stats[:, 0:(T - 1) * 12]).then_inc(y_agg_done, 1)
                nc.vector.bn_aggr(y_agg[:, 1, :], y_stats[:, (T - 1) * 12:(T - 1) * 12 + 6]).then_inc(y_agg_done, 1)
                dve.wait_ge(y_agg_done, 2 * image + 2)

            def variances(layer, image, ph):
                chain, length, at = (x_chain, X_LEN, X_AGG) if layer == 0 else (y_chain, Y_LEN, 0)
                dve.wait_ge(coef_sum, 2 * ph + 1)
                if layer == 0:
                    means, varis, m, n = x_agg[:, :, 0], x_agg[:, :, 1], small[:, 0:G], G
                else:
                    means, varis, m, n = y_agg[:, :, 0], y_agg[:, :, 1], small[:, 0:1], 2
                w = G if layer == 0 else 1
                nc.vector.tensor_copy(c_mean[:, 0:w], m).then_inc(chain, 1)
                at += 1
                dve.wait_ge(chain, length * image + at)
                if layer == 0:
                    nc.vector.tensor_tensor(c_a[:, 0:n], means, c_mean[:, 0:n], ALU.subtract).then_inc(chain, 1)
                else:
                    nc.vector.tensor_scalar(c_a[:, 0:n], means, c_mean[:, 0:1], None,
                                            ALU.subtract).then_inc(chain, 1)
                at += 1
                dve.wait_ge(chain, length * image + at)
                nc.vector.tensor_tensor(c_b[:, 0:n], c_a[:, 0:n], c_a[:, 0:n], ALU.mult).then_inc(chain, 1)
                at += 1
                dve.wait_ge(chain, length * image + at)
                nc.vector.tensor_tensor(c_var[:, 0:n], c_b[:, 0:n], varis, ALU.add).then_inc(chain, 1)

            def coefficients(layer, image, ph, parity):
                chain, length, at = (x_chain, X_LEN, X_VAR) if layer == 0 else (y_chain, Y_LEN, Y_VAR)
                w = G if layer == 0 else 1
                at = [at]

                def link(ins):
                    ins.then_inc(chain, 1)
                    at[0] += 1
                    dve.wait_ge(chain, length * image + at[0])

                dve.wait_ge(coef_sum, 2 * ph + 2)
                v, r, q = c_a[:, 0:w], c_r[:, 0:w], c_b[:, 0:w]
                link(nc.vector.tensor_scalar(v, small[:, G:G + w], EPS, None, ALU.add))
                dve.wait_ge(root_ready, ph + 1)
                link(nc.vector.reciprocal(r, c_r[:, G:G + w]))
                link(nc.vector.tensor_tensor(q, v, r, ALU.mult))
                link(nc.vector.tensor_tensor(c_var[:, 0:w], q, r, ALU.mult))
                link(nc.vector.tensor_scalar(q, c_var[:, 0:w], -0.5, 1.5, ALU.mult, ALU.add))
                if layer == 0:
                    link(nc.vector.tensor_tensor(c_a[:, :], r, q, ALU.mult))
                    link(nc.vector.tensor_tensor(c_b[:, :], c_a[:, :], member, ALU.mult))
                    link(nc.vector.reduce_sum(rstd[:, :], c_b[:, :], AX.X))
                    link(nc.vector.tensor_tensor(c_a[:, :], c_mean[:, :], member, ALU.mult))
                    link(nc.vector.reduce_sum(mean[:, :], c_a[:, :], AX.X))
                    m = mean[:, 0:1]
                else:
                    link(nc.vector.tensor_tensor(rstd[:, :], r, q, ALU.mult))
                    m = c_mean[:, 0:1]
                link(nc.vector.scalar_tensor_tensor(w_scaled[:, :, :], w_band[:, layer], rstd[:, 0:1], center,
                                                    ALU.mult, ALU.add))
                nc.vector.tensor_scalar(shift[:, parity, :], minus, m, None, ALU.mult)
                nc.vector.tensor_tensor(out_bias[:, parity:parity + 1], bias_t[:, layer:layer + 1], m, ALU.add)
                link(nc.vector.tensor_copy(w_hi[:, parity], w_scaled[:, :, :]))
                link(nc.vector.tensor_tensor(w_scaled[:, :, :], w_hi[:, parity].bitcast(f32), center,
                                             ALU.subtract))
                nc.vector.scalar_tensor_tensor(w_lo[:, parity], w_band[:, layer], rstd[:, 0:1],
                                               w_scaled[:, :, :], ALU.mult,
                                               ALU.subtract).then_inc(coef_ready, 1)
                assert at[0] == length, (at[0], length)

            steps(dve, lambda t, j, k: chunk_stats(0, WHOLE, j, k), 0)
            dve.wait_ge(prep, PREP_LEN)
            aggregate_x(0)
            variances(0, 0, 0)
            coefficients(0, 0, 0, 0)

            def output_stats(ph, t, j):
                s = place(j, T)
                dve.wait_ge(out_ready, ph * T + t + 1)
                if j == T - 1:
                    nc.vector.bn_stats(y_stats[:, t * 12:t * 12 + 6],
                                       out_t[:, s, 0:QW]).then_inc(y_stats_done, 1)
                    return
                for h in range(2):
                    nc.vector.bn_stats(y_stats[:, bass.ds(t * 12 + 6 * h, 6)],
                                       out_t[:, s, h * HALF:(h + 1) * HALF]).then_inc(y_stats_done, 1)

            def phase(ph, layer, image, stats, before, after):
                parity = phase_parity(ph, layer)

                def step(t, j, k):
                    s = place(j, T)
                    n = ph * T + t
                    dve.wait_ge(hi_ready, n + 1)
                    for v, a, z, x_a in pieces(j):
                        last = nc.vector.scalar_tensor_tensor(lo[:, s, a:z], x_t[:, s, x_a:x_a + z - a],
                                                              shift[:, parity, v:v + 1],
                                                              hi[:, s, a:z].bitcast(f32), ALU.add, ALU.subtract)
                    last.then_inc(lo_ready, 1)
                    if j >= LAG_STORE:
                        if j == LAG_STORE and before is not None and before[0] == 0:
                            aggregate_y(before[1])
                        if layer == 0:
                            output_stats(ph, t - LAG_STORE, j - LAG_STORE)
                    elif before is not None and before[0] == 0:
                        q = ago(j, LAG_STORE)
                        output_stats(ph - 1, q, q)
                    if stats is not None:
                        chunk_stats(ph + 1, stats[1], j, k)
                    if after is not None:
                        if j == T - 7 and after[0] == 0:
                            aggregate_x(ph + 1)
                        if j == T - 5:
                            variances(after[0], after[1], ph + 1)
                        if j == T - 3:
                            coefficients(after[0], after[1], ph + 1, 1 - parity)

                steps(dve, step, ph)

            phases(dve, phase)

        @block.tensor
        def _(pe):
            def sum_means(layer, image):
                if layer == 0:
                    pe.wait_ge(x_chain, X_LEN * image + X_AGG)
                    nc.tensor.matmul(small[:, 0:G], avg_all, x_agg[:, :, 0], start=True,
                                     stop=True).then_inc(coef_sum, 1)
                else:
                    pe.wait_ge(y_agg_done, 2 * image + 2)
                    nc.tensor.matmul(small[:, 0:1], avg_body, y_agg[:, 0, 0:1], start=True, stop=False)
                    nc.tensor.matmul(small[:, 0:1], avg_last, y_agg[:, 1, 0:1], start=False,
                                     stop=True).then_inc(coef_sum, 1)

            def sum_variances(layer, image):
                if layer == 0:
                    pe.wait_ge(x_chain, X_LEN * image + X_VAR)
                    nc.tensor.matmul(small[:, G:2 * G], avg_all, c_var[:, :], start=True,
                                     stop=True).then_inc(coef_sum, 1)
                else:
                    pe.wait_ge(y_chain, Y_LEN * image + Y_VAR)
                    nc.tensor.matmul(small[:, G:G + 1], avg_body, c_var[:, 0:1], start=True, stop=False)
                    nc.tensor.matmul(small[:, G:G + 1], avg_last, c_var[:, 1:2], start=False,
                                     stop=True).then_inc(coef_sum, 1)

            sum_means(0, 0)
            sum_variances(0, 0)

            def phase(ph, layer, image, stats, before, after):
                parity = phase_parity(ph, layer)
                pe.wait_ge(coef_ready, ph + 1)

                def step(t, j, k):
                    s = place(j, T)
                    n = ph * T + t
                    free = n - 1 if j in (0, 1) else n - 2
                    if positive(free):
                        pe.wait_ge(out_ready, free)
                    pe.wait_ge(lo_ready, n + 1)
                    acc = conv[psum_place(j, T)]
                    terms = [(w, v, kw) for v, w in ((lo, w_hi), (hi, w_lo), (hi, w_hi)) for kw in (0, 2, 1)]
                    kind, columns = (LAST, [(0, QW)]) if j == T - 1 else (BODY, [(0, HALF), (HALF, W)])
                    for i, (w, v, kw) in enumerate(terms):
                        for a, z in columns:
                            last = nc.tensor.matmul(acc[:, a:z],
                                                    w[:, parity, kind, kw * NTAP:(kw + 1) * NTAP],
                                                    v[:, s, a + kw:z + kw],
                                                    start=(i == 0), stop=(i == len(terms) - 1))
                    last.then_inc(conv_done, 1)
                    if after is not None:
                        if j == T - 7:
                            sum_means(*after)
                        if j == T - 5:
                            sum_variances(*after)

                steps(pe, step, ph)

            phases(pe, phase)


def phase_parity(ph, layer):
    if isinstance(ph, int):
        return ph % 2
    return 1 - layer


def kernel(x, L0_conv_weight, L0_conv_bias, L1_conv_weight, L1_conv_bias):
    import concourse.bacc as bacc
    from concourse.bass_utils import run_bass_kernel_spmd

    B, C, H, W = x.shape
    arrays = {
        "x": np.ascontiguousarray(x),
        "w0": np.ascontiguousarray(L0_conv_weight),
        "b0": np.ascontiguousarray(L0_conv_bias),
        "w1": np.ascontiguousarray(L1_conv_weight),
        "b1": np.ascontiguousarray(L1_conv_bias),
        "consts": layout_constants(C, H, W, 4),
    }
    nc = bacc.Bacc("TRN2", target_bir_lowering=False, num_devices=1)
    f32 = mybir.dt.float32
    args = [nc.dram_tensor(n, a.shape, f32, kind="ExternalInput").ap() for n, a in arrays.items()]
    mid = nc.dram_tensor("layer0_out", (B, H, C, W), f32).ap()
    out = nc.dram_tensor("out", (B, C, H, W), f32, kind="ExternalOutput").ap()
    build(nc, *args, mid, out)
    r = run_bass_kernel_spmd(nc, [arrays], core_ids=[0])
    return r.results[0]["out"]
```
